# Optimizing a Trainium2 kernel written in Bass

```python
import numpy as np
import jax
import jax.numpy as jnp

def _softmax(x, axis=-1):
    return jax.nn.softmax(x, axis=axis)

def _gelu(x):
    return jax.nn.gelu(x, approximate=True)

def _silu(x):
    return jax.nn.silu(x)

def _sigmoid(x):
    return jax.nn.sigmoid(x)

def _layernorm(x, axis=-1, eps=1e-05):
    m = jnp.mean(x, axis=axis, keepdims=True)
    v = jnp.var(x, axis=axis, keepdims=True)
    return (x - m) / jnp.sqrt(v + eps)

def _scatter_add(tgt, idx, src, axis=0):
    return tgt.at[idx].add(src)

def _segment_sum(src, seg, n):
    return jax.ops.segment_sum(src, seg, n)
kernel_name = 'mk_rec_standalone_d1_rec_r8_43c53f'

def setup_inputs(seed: int=0):
    np.random.seed(seed)
    _w = jnp.asarray

    def _rec_inputs():
        import jax
        import jax.numpy as jnp
        _rk = jax.random.key(seed)
        r_x = jax.random.randint(jax.random.fold_in(_rk, 1), (512, 2500), 0, 2, jnp.int32)
        return r_x
    r_x = _rec_inputs()

    def _L0_rec_setup():
        import jax, jax.numpy as jnp
        import numpy as np
        BN_EPS = 1e-05

        def _batchnorm(h, gamma, beta):
            mean = jnp.mean(h, axis=0)
            var = jnp.var(h, axis=0)
            return gamma * (h - mean) * jax.lax.rsqrt(var + BN_EPS) + beta
        key = jax.random.key(seed)
        k = jax.random.split(key, 4)
        B, V, D, L, OUT = (512, 2500, 128, 4, 25)
        x = jax.random.randint(k[0], (B, V), 0, 2, dtype=jnp.int32)
        emb = jax.random.normal(k[1], (V, D), dtype=jnp.float32)
        Ws = jax.random.normal(k[2], (L, D, D), dtype=jnp.float32) / np.sqrt(D)
        bs = jnp.zeros((L, D), jnp.float32)
        gammas = jnp.ones((L, D), jnp.float32)
        betas = jnp.zeros((L, D), jnp.float32)
        fcW = jax.random.normal(k[3], (D, OUT), dtype=jnp.float32) / np.sqrt(D)
        fcb = jnp.zeros((OUT,), jnp.float32)
        return {'x': x, 'emb': emb, 'Ws': Ws, 'bs': bs, 'gammas': gammas, 'betas': betas, 'fcW': fcW, 'fcb': fcb}
    _L0_rec_all = _L0_rec_setup()
    _L0_rec_in = {k: v for k, v in _L0_rec_all.items() if k in ('emb', 'Ws', 'bs', 'gammas', 'betas', 'fcW', 'fcb')}
    del _L0_rec_all
    return {'r_x': r_x, 'L0_rec_emb': _L0_rec_in['emb'], 'L0_rec_Ws': _L0_rec_in['Ws'], 'L0_rec_bs': _L0_rec_in['bs'], 'L0_rec_gammas': _L0_rec_in['gammas'], 'L0_rec_betas': _L0_rec_in['betas'], 'L0_rec_fcW': _L0_rec_in['fcW'], 'L0_rec_fcb': _L0_rec_in['fcb']}

def reference(r_x, L0_rec_emb, L0_rec_Ws, L0_rec_bs, L0_rec_gammas, L0_rec_betas, L0_rec_fcW, L0_rec_fcb):
    import jax
    import jax.numpy as jnp

    def _L0_rec_ref(x, emb, Ws, bs, gammas, betas, fcW, fcb):
        import jax, jax.numpy as jnp
        import numpy as np
        BN_EPS = 1e-05

        def _batchnorm(h, gamma, beta):
            mean = jnp.mean(h, axis=0)
            var = jnp.var(h, axis=0)
            return gamma * (h - mean) * jax.lax.rsqrt(var + BN_EPS) + beta
        h = jnp.einsum('bv,vd->bd', x.astype(emb.dtype), emb)
        for i in range(Ws.shape[0]):
            h = h @ Ws[i] + bs[i]
            h = jax.nn.relu(h)
            h = _batchnorm(h, gammas[i], betas[i])
        return h @ fcW + fcb
    y = _L0_rec_ref(r_x, L0_rec_emb, L0_rec_Ws, L0_rec_bs, L0_rec_gammas, L0_rec_betas, L0_rec_fcW, L0_rec_fcb)
    return y

_drawn_inputs = setup_inputs


def setup_inputs(seed=0):
    import zlib

    import numpy as np

    out = dict(_drawn_inputs(seed))
    spreads = {'L0_rec_bs': (0.0, 0.1),
     'L0_rec_gammas': (1.0, 0.2),
     'L0_rec_betas': (0.0, 0.1),
     'L0_rec_fcb': (0.0, 0.1)}
    factors = {}
    for name, (base, spread) in spreads.items():
        noise = np.random.default_rng([zlib.crc32(name.encode()), seed]).standard_normal(out[name].shape)
        drawn = base * np.exp(spread * noise) if base else spread * noise
        out[name] = jnp.asarray(drawn.astype(out[name].dtype))
    for name, factor in factors.items():
        out[name] = (out[name] * factor).astype(out[name].dtype)
    return out
```

```python
import numpy as np

import concourse.bass as bass
from concourse import mybir

B, V, D, L, OUT = 512, 2500, 128, 4, 25
P = 128
EPS = 1e-5

FULL = V // P
REST = V - FULL * P
TILES = FULL + 1
REST_MAIN = REST // 16 * 16
CHUNKS = [1, 1, 2, 3, 4, 4, 4]
assert sum(CHUNKS) == FULL
SHORT_AFTER = 4

HALVES = [(0, 256), (256, 512)]
BC = B // P

COL_W = 0
COL_B = L * D
COL_GAMMA = COL_B + L
COL_BETA = COL_GAMMA + L
COL_FCW = COL_BETA + L
PARAM_COLS = COL_FCW + OUT


def build(nc, x_main, x_rest, emb_main, emb_rest, w_first, params, fcb, out):
    f32, i32, bf16 = mybir.dt.float32, mybir.dt.int32, mybir.dt.bfloat16
    ALU = mybir.AluOpType
    ACT = mybir.ActivationFunctionType

    from contextlib import ExitStack
    ctx = ExitStack()
    with ctx:
        def sbuf(name, shape, dt=f32):
            return ctx.enter_context(nc.sbuf_tensor(name, shape, dt))

        def psum(name, shape):
            return ctx.enter_context(nc.psum_tensor(name, shape, f32))

        def sem(name):
            return ctx.enter_context(nc.semaphore(name))

        x_int = sbuf("x_int", [P, TILES, B], i32)
        x_f32 = sbuf("x_f32", [P, TILES, B])
        emb_sb = sbuf("emb_sb", [P, TILES, D])
        w0_sb = sbuf("w0_sb", [P, D])
        params_sb = sbuf("params_sb", [P, PARAM_COLS])
        fcb_sb = sbuf("fcb_sb", [P, OUT])
        emb_sum = sbuf("emb_sum", [D, B])
        h_sb = sbuf("h_sb", [D, L, B])
        stats = sbuf("stats", [D, L, 2, 6])
        moments = sbuf("moments", [D, L, 2])
        std = sbuf("std", [D, L])
        rstd = sbuf("rstd", [D, L])
        w_scaled = sbuf("w_scaled", [D, L, D])
        fcw_scaled = sbuf("fcw_scaled", [D, OUT])
        beta_bias = sbuf("beta_bias", [D, L])
        bias = sbuf("bias", [D, L])
        fc_beta_bias = sbuf("fc_beta_bias", [P, OUT])
        fc_bias = sbuf("fc_bias", [P, OUT])
        y_sb = sbuf("y_sb", [P, BC, OUT])
        eps_sb = sbuf("eps_sb", [P, 1])
        warm = sbuf("warm", [P, B], bf16)

        acc = [psum("acc0", [P, 512]), psum("acc1", [P, 512])]
        z = [psum("z0", [P, 512]), psum("z1", [P, 512])]
        ps_beta = psum("ps_beta", [P, 512])
        ps_mean = psum("ps_mean", [P, 512])
        ps_y = psum("ps_y", [P, 512])

        x_loaded = [sem(f"x_loaded{c}") for c in range(len(CHUNKS))]
        emb_loaded = [sem(f"emb_loaded{c}") for c in range(2)]
        rest_loaded = sem("rest_loaded")
        emb_rest_loaded = sem("emb_rest_loaded")
        w0_loaded = sem("w0_loaded")
        params_loaded = sem("params_loaded")
        fcb_loaded = sem("fcb_loaded")
        eps_set = sem("eps_set")
        warm_set = sem("warm_set")
        x_cast = sem("x_cast")
        acc_done = sem("acc_done")
        sum_copied = [sem("sum_copied0"), sem("sum_copied1")]
        z_done = [sem("z_done0"), sem("z_done1")]
        relu_done = [sem("relu_done0"), sem("relu_done1")]
        stats_done = sem("stats_done")
        moments_done = sem("moments_done")
        std_done = sem("std_done")
        rstd_done = sem("rstd_done")
        w_ready = sem("w_ready")
        mean_product = sem("mean_product")
        beta_product = sem("beta_product")
        beta_bias_ready = sem("beta_bias_ready")
        bias_ready = sem("bias_ready")
        y_product = sem("y_product")
        y_ready = sem("y_ready")
        out_stored = sem("out_stored")

        starts = [sum(CHUNKS[:c]) for c in range(len(CHUNKS))]
        order, chunk_of = [], {}
        for c, n in enumerate(CHUNKS):
            for t in range(starts[c], starts[c] + n):
                order.append(t)
                chunk_of[t] = c
            if c == SHORT_AFTER - 1:
                order.append(FULL)

        def rows(t):
            return REST if t == FULL else P

        def w_raw(layer):
            return params_sb[:, COL_W + layer * D:COL_W + (layer + 1) * D]

        def param(col, layer):
            return params_sb[:, col + layer:col + layer + 1]

        EMB_SPLIT = 4

        block = ctx.enter_context(nc.Block())

        @block.sync
        def _(sp):
            sp.dma_start(emb_sb[:, 0:EMB_SPLIT, :], emb_main[:, 0:EMB_SPLIT, :]).then_inc(emb_loaded[0], 16)
            for c, n in enumerate(CHUNKS):
                t = starts[c]
                sp.dma_start(x_int[:, t:t + n, :], x_main[:, t:t + n, :]).then_inc(x_loaded[c], 16)
                if c == 1:
                    sp.dma_start(emb_sb[:, EMB_SPLIT:FULL, :], emb_main[:, EMB_SPLIT:FULL, :]).then_inc(emb_loaded[1], 16)
            sp.dma_start(params_sb[:, :], params[:, :]).then_inc(params_loaded, 16)
            sp.dma_start(fcb_sb[:, :], fcb.partition_broadcast(P)).then_inc(fcb_loaded, 16)
            sp.wait_ge(y_ready, 1)
            sp.dma_start(out.rearrange("(p c) n -> p (c n)", c=BC), y_sb[:, :, :].rearrange("p c n -> p (c n)")).then_inc(out_stored, 16)
            sp.wait_ge(out_stored, 16)

        @block.gpsimd
        def _(pool):
            nc.gpsimd.memset(eps_sb[:, :], EPS).then_inc(eps_set, 1)

        @block.scalar
        def _(act):
            act.dma_start(x_int[0:REST_MAIN, FULL, :], x_rest[0:REST_MAIN, :]).then_inc(rest_loaded, 16)
            act.dma_start(x_int[REST_MAIN:REST, FULL, :], x_rest[REST_MAIN:REST, :]).then_inc(rest_loaded, 16)
            act.dma_start(emb_sb[0:REST_MAIN, FULL, :], emb_rest[0:REST_MAIN, :]).then_inc(emb_rest_loaded, 16)
            act.dma_start(emb_sb[REST_MAIN:REST, FULL, :], emb_rest[REST_MAIN:REST, :]).then_inc(emb_rest_loaded, 16)
            act.dma_start(w0_sb[:, :], w_first[:, :]).then_inc(w0_loaded, 16)

            act.wait_ge(acc_done, 2)
            lo, hi = HALVES[1]
            nc.scalar.activation(emb_sum[:, lo:hi], acc[1][:, 0:hi - lo], ACT.Copy).then_inc(sum_copied[1], 1)

            act.wait_ge(params_loaded, 16)
            act.wait_ge(eps_set, 1)
            for layer in range(L):
                act.wait_ge(z_done[1], layer + 1)
                if layer > 0:
                    act.wait_ge(bias_ready, layer)
                nc.scalar.activation(h_sb[:, layer, lo:hi], z[1][:, 0:hi - lo], ACT.Relu,
                                     bias=param(COL_B, 0) if layer == 0 else bias[:, layer:layer + 1]).then_inc(relu_done[1], 1)
                if layer < L - 1:
                    act.wait_ge(beta_product, layer + 1)
                    nc.scalar.activation(beta_bias[:, layer + 1:layer + 2], ps_beta[:, 0:1], ACT.Identity,
                                         bias=param(COL_B, layer + 1)).then_inc(beta_bias_ready, 1)
                act.wait_ge(moments_done, layer + 1)
                nc.scalar.activation(std[:, layer:layer + 1], moments[:, layer, 1:2], ACT.Sqrt,
                                     bias=eps_sb[:, :]).then_inc(std_done, 1)

        @block.vector
        def _(dve):
            nc.vector.memset(warm[:, :], 0.0).then_inc(warm_set, 1)
            for t in order:
                if t == FULL:
                    dve.wait_ge(rest_loaded, 32)
                else:
                    dve.wait_ge(x_loaded[chunk_of[t]], 16)
                nc.vector.tensor_copy(x_f32[0:rows(t), t, :], x_int[0:rows(t), t, :]).then_inc(x_cast, 1)

            dve.wait_ge(acc_done, 1)
            lo, hi = HALVES[0]
            nc.vector.tensor_copy(emb_sum[:, lo:hi], acc[0][:, 0:hi - lo]).then_inc(sum_copied[0], 1)

            dve.wait_ge(params_loaded, 16)
            for layer in range(L):
                if layer > 0:
                    dve.wait_ge(mean_product, layer)
                    dve.wait_ge(beta_bias_ready, layer)
                    nc.vector.tensor_tensor(bias[:, layer:layer + 1], beta_bias[:, layer:layer + 1],
                                            ps_mean[:, 0:1], ALU.subtract).then_inc(bias_ready, 1)
                    dve.wait_ge(bias_ready, layer)
                dve.wait_ge(z_done[0], layer + 1)
                nc.vector.tensor_scalar(h_sb[:, layer, lo:hi], z[0][:, 0:hi - lo],
                                        param(COL_B, 0) if layer == 0 else bias[:, layer:layer + 1], 0.0,
                                        ALU.add, ALU.max).then_inc(relu_done[0], 1)
                for half, (a, b) in enumerate(HALVES):
                    dve.wait_ge(relu_done[half], layer + 1)
                    nc.vector.bn_stats(stats[:, layer, half, :], h_sb[:, layer, a:b]).then_inc(stats_done, 1)
                dve.wait_ge(stats_done, 2 * (layer + 1))
                nc.vector.bn_aggr(moments[:, layer, :], stats[:, layer, :, :]).then_inc(moments_done, 1)
                dve.wait_ge(std_done, layer + 1)
                nc.vector.reciprocal(rstd[:, layer:layer + 1], std[:, layer:layer + 1]).then_inc(rstd_done, 1)
                dve.wait_ge(rstd_done, layer + 1)
                if layer < L - 1:
                    dst, src = w_scaled[:, layer + 1, :], w_raw(layer + 1)
                else:
                    dst, src = fcw_scaled[:, :], params_sb[:, COL_FCW:COL_FCW + OUT]
                nc.vector.tensor_scalar(dst, src, rstd[:, layer:layer + 1], param(COL_GAMMA, layer),
                                        ALU.mult, ALU.mult).then_inc(w_ready, 1)
                if layer == L - 2:
                    dve.wait_ge(beta_product, L)
                    dve.wait_ge(fcb_loaded, 16)
                    nc.vector.tensor_tensor(fc_beta_bias[:, :], fcb_sb[:, :], ps_beta[:, 0:OUT],
                                            ALU.add).then_inc(beta_bias_ready, 1)
            dve.wait_ge(mean_product, L)
            dve.wait_ge(beta_bias_ready, L)
            nc.vector.tensor_tensor(fc_bias[:, :], fc_beta_bias[:, :], ps_mean[:, 0:OUT],
                                    ALU.subtract).then_inc(bias_ready, 1)
            dve.wait_ge(bias_ready, L)
            dve.wait_ge(y_product, 1)
            nc.vector.tensor_tensor(y_sb[:, :, :], ps_y[:, 0:BC * OUT].rearrange("p (c n) -> p c n", c=BC),
                                    fc_bias[:, :].unsqueeze(1).broadcast_to([P, BC, OUT]),
                                    ALU.add).then_inc(y_ready, 1)

        @block.tensor
        def _(pe):
            pe.wait_ge(warm_set, 1)
            for _i in range(6):
                nc.tensor.matmul(ps_y[:, :], warm[:, 0:P], warm[:, :], start=True, stop=True)

            tail = order[-CHUNKS[-1]:]
            steps = [(t, half) for t in order[:-CHUNKS[-1]] for half in range(2)]
            steps += [(t, half) for half in range(2) for t in tail]
            for t, half in steps:
                i = order.index(t)
                a, b = HALVES[half]
                pe.wait_ge(x_cast, i + 1)
                if t == FULL:
                    pe.wait_ge(emb_rest_loaded, 32)
                else:
                    pe.wait_ge(emb_loaded[0 if t < EMB_SPLIT else 1], 16)
                done = nc.tensor.matmul(acc[half][:, 0:b - a], emb_sb[0:rows(t), t, :], x_f32[0:rows(t), t, a:b],
                                        start=i == 0, stop=i == TILES - 1)
                if i == TILES - 1:
                    done.then_inc(acc_done, 1)

            for layer in range(L):
                if layer == 0:
                    pe.wait_ge(w0_loaded, 16)
                    weights, source = w0_sb[:, :], emb_sum
                else:
                    weights, source = w_scaled[:, layer, :], h_sb[:, layer - 1, :]
                    pe.wait_ge(w_ready, layer)
                    nc.tensor.matmul(ps_mean[:, 0:1], weights, moments[:, layer - 1, 0:1],
                                     start=True, stop=True).then_inc(mean_product, 1)
                for half, (a, b) in enumerate(HALVES):
                    if layer == 0:
                        pe.wait_ge(sum_copied[half], 1)
                    nc.tensor.matmul(z[half][:, 0:b - a], weights, source[:, a:b],
                                     start=True, stop=True).then_inc(z_done[half], 1)
                if layer == 0:
                    pe.wait_ge(params_loaded, 16)
                else:
                    pe.wait_ge(beta_bias_ready, layer)
                if layer < L - 1:
                    nc.tensor.matmul(ps_beta[:, 0:1], w_raw(layer + 1), param(COL_BETA, layer),
                                     start=True, stop=True).then_inc(beta_product, 1)
                else:
                    nc.tensor.matmul(ps_beta[:, 0:OUT], param(COL_BETA, layer).broadcast_to([D, P]),
                                     params_sb[:, COL_FCW:COL_FCW + OUT], start=True, stop=True).then_inc(beta_product, 1)

            pe.wait_ge(w_ready, L)
            nc.tensor.matmul(ps_mean[:, 0:OUT], moments[:, L - 1, 0:1].broadcast_to([D, P]), fcw_scaled[:, :],
                             start=True, stop=True).then_inc(mean_product, 1)
            for c in range(BC):
                done = nc.tensor.matmul(ps_y[:, c * OUT:(c + 1) * OUT], h_sb[:, L - 1, c * P:(c + 1) * P],
                                        fcw_scaled[:, :], start=True, stop=True)
            done.then_inc(y_product, 1)


def kernel(r_x, L0_rec_emb, L0_rec_Ws, L0_rec_bs, L0_rec_gammas, L0_rec_betas, L0_rec_fcW, L0_rec_fcb):
    import concourse.bacc as bacc
    from concourse.bass_utils import run_bass_kernel_spmd

    x_t = np.asarray(r_x).reshape(P, BC, V).transpose(2, 1, 0).reshape(V, B)
    emb = np.asarray(L0_rec_emb)
    ws = np.asarray(L0_rec_Ws)
    arrays = {
        "x_main": np.ascontiguousarray(x_t[:FULL * P].reshape(P, FULL, B)),
        "x_rest": np.ascontiguousarray(x_t[FULL * P:]),
        "emb_main": np.ascontiguousarray(emb[:FULL * P].reshape(P, FULL, D)),
        "emb_rest": np.ascontiguousarray(emb[FULL * P:]),
        "w_first": np.ascontiguousarray(ws[0]),
        "params": np.ascontiguousarray(np.concatenate(
            [ws.transpose(1, 0, 2).reshape(D, L * D), np.asarray(L0_rec_bs).T, np.asarray(L0_rec_gammas).T,
             np.asarray(L0_rec_betas).T, np.asarray(L0_rec_fcW)], axis=1)),
        "fcb": np.ascontiguousarray(np.asarray(L0_rec_fcb)),
    }
    nc = bacc.Bacc("TRN2", target_bir_lowering=False, num_devices=1)
    ins = {k: nc.dram_tensor(k, a.shape, mybir.dt.from_np(a.dtype), kind="ExternalInput").ap()
           for k, a in arrays.items()}
    out = nc.dram_tensor("out", (B, OUT), mybir.dt.float32, kind="ExternalOutput").ap()
    build(nc, out=out, **ins)
    result = run_bass_kernel_spmd(nc, [arrays], core_ids=[0])
    return result.results[0]["out"]
```

```python
from contextlib import ExitStack

import numpy as np

from concourse import mybir

B, V, D, L, OUT = 512, 2500, 128, 4, 25
P = 128
EPS = 1e-5

FULL = V // P
REST = V - FULL * P
TILES = FULL + 1
SHORT = FULL
REST_MAIN = REST // 16 * 16
X_CHUNKS = [1] * 19
EMB_CHUNKS = [1, 2, 3, 3, 5, 5]
assert sum(X_CHUNKS) == FULL and sum(EMB_CHUNKS) == FULL
EMB_BEFORE = [0, 1, 3, 5, 7, 10]
SHORT_AFTER = 7

COLS = [(0, 128), (128, 320), (320, 512)]
ON_DVE = [True, False, False]
BC = B // P

WARM_START = 9
WARM_LAYER = 6

COL_W = 0
COL_FCW = COL_W + (L - 1) * D
COL_B = COL_FCW + OUT
COL_GAMMA = COL_B + L
COL_BETA = COL_GAMMA + L
PARAM_COLS = COL_BETA + L


def first_tiles(sizes):
    return [sum(sizes[:n]) for n in range(len(sizes))]


def build(nc, x_main, x_rest, emb_main, emb_rest, w_first, params, fcb, out):
    f32, i32, bf16 = mybir.dt.float32, mybir.dt.int32, mybir.dt.bfloat16
    ALU = mybir.AluOpType
    ACT = mybir.ActivationFunctionType
    PARTS = len(COLS)

    x_starts, emb_starts = first_tiles(X_CHUNKS), first_tiles(EMB_CHUNKS)
    order = list(range(SHORT_AFTER)) + [SHORT] + list(range(SHORT_AFTER, FULL))
    x_chunk = {t: c for c, n in enumerate(X_CHUNKS) for t in range(x_starts[c], x_starts[c] + n)}
    emb_chunk = {t: c for c, n in enumerate(EMB_CHUNKS) for t in range(emb_starts[c], emb_starts[c] + n)}

    def rows(t):
        return REST if t == SHORT else P

    ctx = ExitStack()
    with ctx:
        def sbuf(name, shape, dt=f32):
            return ctx.enter_context(nc.sbuf_tensor(name, shape, dt))

        def bank(name):
            return ctx.enter_context(nc.psum_tensor(name, [P, 512], f32))

        def sem(name):
            return ctx.enter_context(nc.semaphore(name))

        x_int = sbuf("x_int", [P, TILES, B], i32)
        x_f32 = sbuf("x_f32", [P, TILES, B])
        emb_sb = sbuf("emb_sb", [P, TILES, D])
        w0_sb = sbuf("w0_sb", [D, D])
        params_sb = sbuf("params_sb", [D, PARAM_COLS])
        fcb_sb = sbuf("fcb_sb", [P, OUT])
        emb_sum = sbuf("emb_sum", [D, B])
        h_sb = sbuf("h_sb", [D, L, B])
        centred = sbuf("centred", [D, L, B])
        stats = sbuf("stats", [D, L, PARTS, 6])
        moments = sbuf("moments", [D, L, 2])
        std = sbuf("std", [D, L])
        rstd = sbuf("rstd", [D, L])
        w_gamma = sbuf("w_gamma", [D, COL_B])
        w_scaled = sbuf("w_scaled", [D, COL_B])
        bias = sbuf("bias", [D, L])
        fc_bias = sbuf("fc_bias", [P, OUT])
        y_sb = sbuf("y_sb", [P, BC, OUT])
        eps_sb = sbuf("eps_sb", [P, 1])
        scratch = sbuf("scratch", [P, 1])

        z = [bank(f"z{j}") for j in range(PARTS)]
        ps_beta = bank("ps_beta")
        ps_y = bank("ps_y")

        x_loaded = [sem(f"x_loaded{c}") for c in range(len(X_CHUNKS))]
        emb_loaded = [sem(f"emb_loaded{c}") for c in range(len(EMB_CHUNKS))]
        x_rest_loaded = sem("x_rest_loaded")
        emb_rest_loaded = sem("emb_rest_loaded")
        w0_loaded = sem("w0_loaded")
        params_loaded = sem("params_loaded")
        fcb_loaded = sem("fcb_loaded")
        eps_set = sem("eps_set")
        x_cast = sem("x_cast")
        acc_done = [sem(f"acc_done{j}") for j in range(PARTS)]
        sum_copied = [sem(f"sum_copied{j}") for j in range(PARTS)]
        gamma_ready = sem("gamma_ready")
        z_done = [sem(f"z_done{j}") for j in range(PARTS)]
        relu_done = [sem(f"relu_done{j}") for j in range(PARTS)]
        stats_done = sem("stats_done")
        moments_done = sem("moments_done")
        centred_done = sem("centred_done")
        std_done = sem("std_done")
        rstd_done = sem("rstd_done")
        w_ready = sem("w_ready")
        beta_product = sem("beta_product")
        bias_ready = sem("bias_ready")
        y_product = sem("y_product")
        y_ready = sem("y_ready")
        out_stored = sem("out_stored")

        def weight_cols(layer):
            return (layer * D, (layer + 1) * D) if layer < L - 1 else (COL_FCW, COL_FCW + OUT)

        def param(col, layer):
            return params_sb[:, col + layer:col + layer + 1]

        def bias_of(layer):
            return param(COL_B, 0) if layer == 0 else bias[:, layer:layer + 1]

        ones = nc.const_aps.tensor(1.0, [P, 512], bf16)

        block = ctx.enter_context(nc.Block())

        @block.sync
        def _(sp):
            for c, n in enumerate(X_CHUNKS):
                for e, m in enumerate(EMB_CHUNKS):
                    if EMB_BEFORE[e] == c:
                        t = emb_starts[e]
                        sp.dma_start(emb_sb[:, t:t + m, :], emb_main[:, t:t + m, :]).then_inc(emb_loaded[e], 16)
                t = x_starts[c]
                sp.dma_start(x_int[:, t:t + n, :], x_main[:, t:t + n, :]).then_inc(x_loaded[c], 16)
            sp.dma_start(params_sb[:, :], params[:, :]).then_inc(params_loaded, 16)
            sp.dma_start(fcb_sb[:, :], fcb.partition_broadcast(P)).then_inc(fcb_loaded, 16)
            sp.wait_ge(y_ready, 1)
            sp.dma_start(out.rearrange("(p c) n -> p (c n)", c=BC),
                         y_sb[:, :, :].rearrange("p c n -> p (c n)")).then_inc(out_stored, 16)
            sp.wait_ge(out_stored, 16)

        @block.gpsimd
        def _(pool):
            nc.gpsimd.memset(eps_sb[:, :], EPS).then_inc(eps_set, 1)
            pool.wait_ge(params_loaded, 16)
            for layer in range(L):
                a, b = weight_cols(layer)
                nc.gpsimd.tensor_scalar(w_gamma[:, a:b], params_sb[:, a:b], param(COL_GAMMA, layer), None,
                                        ALU.mult).then_inc(gamma_ready, 1)

        @block.scalar
        def _(act):
            act.wait_ge(eps_set, 1)
            nc.scalar.activation(scratch[:, :], eps_sb[:, :], ACT.Sqrt)
            act.wait_ge(x_loaded[1], 16)
            for sb, dram, done in ((emb_sb, emb_rest, emb_rest_loaded), (x_int, x_rest, x_rest_loaded)):
                act.dma_start(sb[0:REST_MAIN, SHORT, :], dram[0:REST_MAIN, :]).then_inc(done, 16)
                act.dma_start(sb[REST_MAIN:REST, SHORT, :], dram[REST_MAIN:REST, :]).then_inc(done, 16)
            act.dma_start(w0_sb[:, :], w_first[:, :]).then_inc(w0_loaded, 16)

            for j, (a, b) in enumerate(COLS):
                if not ON_DVE[j]:
                    act.wait_ge(acc_done[j], 1)
                    nc.scalar.activation(emb_sum[:, a:b], z[j][:, 0:b - a], ACT.Copy).then_inc(sum_copied[j], 1)

            act.wait_ge(params_loaded, 16)
            for layer in range(L):
                for j, (a, b) in enumerate(COLS):
                    if not ON_DVE[j]:
                        act.wait_ge(z_done[j], layer + 1)
                        nc.scalar.activation(h_sb[:, layer, a:b], z[j][:, 0:b - a], ACT.Relu,
                                             bias=bias_of(layer)).then_inc(relu_done[j], 1)
                if layer < L - 1:
                    act.wait_ge(beta_product, layer + 1)
                    nc.scalar.activation(bias[:, layer + 1:layer + 2], ps_beta[:, 0:1], ACT.Identity,
                                         bias=param(COL_B, layer + 1)).then_inc(bias_ready, 1)
                    act.wait_ge(bias_ready, layer + 1)
                act.wait_ge(moments_done, layer + 1)
                nc.scalar.activation(std[:, layer:layer + 1], moments[:, layer, 1:2], ACT.Sqrt,
                                     bias=eps_sb[:, :]).then_inc(std_done, 1)

        @block.vector
        def _(dve):
            for t in order:
                if t == SHORT:
                    dve.wait_ge(x_rest_loaded, 32)
                else:
                    dve.wait_ge(x_loaded[x_chunk[t]], 16)
                for a, b in COLS if t == order[-1] else [(0, B)]:
                    nc.vector.tensor_copy(x_f32[0:rows(t), t, a:b], x_int[0:rows(t), t, a:b]).then_inc(x_cast, 1)
            for j, (a, b) in enumerate(COLS):
                if ON_DVE[j]:
                    dve.wait_ge(acc_done[j], 1)
                    nc.vector.tensor_copy(emb_sum[:, a:b], z[j][:, 0:b - a]).then_inc(sum_copied[j], 1)

            dve.wait_ge(params_loaded, 16)
            for layer in range(L):
                if layer > 0:
                    dve.wait_ge(bias_ready, layer)
                for j, (a, b) in enumerate(COLS):
                    if ON_DVE[j]:
                        dve.wait_ge(z_done[j], layer + 1)
                        nc.vector.tensor_scalar(h_sb[:, layer, a:b], z[j][:, 0:b - a], bias_of(layer), 0.0,
                                                ALU.add, ALU.max).then_inc(relu_done[j], 1)
                for j, (a, b) in enumerate(COLS):
                    dve.wait_ge(relu_done[j], layer + 1)
                    nc.vector.bn_stats(stats[:, layer, j, :], h_sb[:, layer, a:b]).then_inc(stats_done, 1)
                dve.wait_ge(stats_done, PARTS * (layer + 1))
                nc.vector.bn_aggr(moments[:, layer, :], stats[:, layer, :, :]).then_inc(moments_done, 1)
                dve.wait_ge(moments_done, layer + 1)
                nc.vector.tensor_scalar(centred[:, layer, :], h_sb[:, layer, :], moments[:, layer, 0:1], None,
                                        ALU.subtract).then_inc(centred_done, 1)
                dve.wait_ge(std_done, layer + 1)
                nc.vector.reciprocal(rstd[:, layer:layer + 1], std[:, layer:layer + 1]).then_inc(rstd_done, 1)
                dve.wait_ge(rstd_done, layer + 1)
                dve.wait_ge(gamma_ready, layer + 1)
                a, b = weight_cols(layer)
                nc.vector.tensor_scalar(w_scaled[:, a:b], w_gamma[:, a:b], rstd[:, layer:layer + 1], None,
                                        ALU.mult).then_inc(w_ready, 1)
            dve.wait_ge(beta_product, L)
            dve.wait_ge(fcb_loaded, 16)
            nc.vector.tensor_tensor(fc_bias[:, :], fcb_sb[:, :], ps_beta[:, 0:OUT], ALU.add).then_inc(bias_ready, 1)
            dve.wait_ge(bias_ready, L)
            dve.wait_ge(y_product, 1)
            nc.vector.tensor_tensor(y_sb[:, :, :], ps_y[:, 0:BC * OUT].rearrange("p (c n) -> p c n", c=BC),
                                    fc_bias[:, :].unsqueeze(1).broadcast_to([P, BC, OUT]),
                                    ALU.add).then_inc(y_ready, 1)

        @block.tensor
        def _(pe):
            def keep_warm(n):
                for _ in range(n):
                    nc.tensor.matmul(ps_y[:, :], ones[:, 0:P], ones,
                                     start=True, stop=True)

            keep_warm(WARM_START)

            for i, t in enumerate(order):
                pe.wait_ge(x_cast, i + 1)
                if t == SHORT:
                    pe.wait_ge(emb_rest_loaded, 32)
                else:
                    pe.wait_ge(emb_loaded[emb_chunk[t]], 16)
                for j, (a, b) in enumerate(COLS):
                    if i == TILES - 1:
                        pe.wait_ge(x_cast, i + 1 + j)
                    done = nc.tensor.matmul(z[j][:, 0:b - a], emb_sb[0:rows(t), t, :], x_f32[0:rows(t), t, a:b],
                                            start=i == 0, stop=i == TILES - 1)
                    if i == TILES - 1:
                        done.then_inc(acc_done[j], 1)

            for layer in range(L):
                if layer == 0:
                    pe.wait_ge(w0_loaded, 16)
                    weights, source = w0_sb[:, :], emb_sum
                else:
                    a, b = weight_cols(layer - 1)
                    weights, source = w_scaled[:, a:b], centred[:, layer - 1, :]
                    pe.wait_ge(centred_done, layer)
                    pe.wait_ge(w_ready, layer)
                for j, (a, b) in enumerate(COLS):
                    if layer == 0:
                        pe.wait_ge(sum_copied[j], 1)
                    nc.tensor.matmul(z[j][:, 0:b - a], weights, source[:, a:b],
                                     start=True, stop=True).then_inc(z_done[j], 1)
                a, b = weight_cols(layer)
                if layer == 0:
                    pe.wait_ge(params_loaded, 16)
                else:
                    pe.wait_ge(bias_ready, layer)
                if layer < L - 1:
                    nc.tensor.matmul(ps_beta[:, 0:1], params_sb[:, a:b], param(COL_BETA, layer),
                                     start=True, stop=True).then_inc(beta_product, 1)
                else:
                    nc.tensor.matmul(ps_beta[:, 0:OUT], param(COL_BETA, layer).broadcast_to([D, P]),
                                     params_sb[:, a:b], start=True, stop=True).then_inc(beta_product, 1)
                keep_warm(WARM_LAYER)

            pe.wait_ge(centred_done, L)
            pe.wait_ge(w_ready, L)
            for c in range(BC):
                done = nc.tensor.matmul(ps_y[:, c * OUT:(c + 1) * OUT], centred[:, L - 1, c * P:(c + 1) * P],
                                        w_scaled[:, COL_FCW:COL_FCW + OUT], start=True, stop=True)
            done.then_inc(y_product, 1)


def kernel(r_x, L0_rec_emb, L0_rec_Ws, L0_rec_bs, L0_rec_gammas, L0_rec_betas, L0_rec_fcW, L0_rec_fcb):
    import concourse.bacc as bacc
    from concourse.bass_utils import run_bass_kernel_spmd

    x_t = np.asarray(r_x).reshape(P, BC, V).transpose(2, 1, 0).reshape(V, B)
    emb, ws = np.asarray(L0_rec_emb), np.asarray(L0_rec_Ws)
    arrays = {
        "x_main": x_t[:FULL * P].reshape(P, FULL, B),
        "x_rest": x_t[FULL * P:],
        "emb_main": emb[:FULL * P].reshape(P, FULL, D),
        "emb_rest": emb[FULL * P:],
        "w_first": ws[0],
        "params": np.concatenate(
            [ws[1:].transpose(1, 0, 2).reshape(D, (L - 1) * D), np.asarray(L0_rec_fcW), np.asarray(L0_rec_bs).T,
             np.asarray(L0_rec_gammas).T, np.asarray(L0_rec_betas).T], axis=1),
        "fcb": np.asarray(L0_rec_fcb),
    }
    arrays = {name: np.ascontiguousarray(a) for name, a in arrays.items()}
    nc = bacc.Bacc("TRN2", target_bir_lowering=False, num_devices=1)
    ins = {name: nc.dram_tensor(name, a.shape, mybir.dt.from_np(a.dtype), kind="ExternalInput").ap()
           for name, a in arrays.items()}
    out = nc.dram_tensor("out", (B, OUT), mybir.dt.float32, kind="ExternalOutput").ap()
    build(nc, out=out, **ins)
    result = run_bass_kernel_spmd(nc, [arrays], core_ids=[0])
    return result.results[0]["out"]
```

```python
from contextlib import ExitStack

import numpy as np

from concourse import mybir

B, V, D, L, OUT = 512, 2500, 128, 4, 25
P = 128
EPS = 1e-5

FULL = V // P
REST = V - FULL * P
SHORT_ROWS = -(-REST // 16) * 16
TILES = FULL + 1
EMB_CHUNKS = [3, 3, 3, 3, 2, 2, 1, 1, 1, 1]
assert sum(EMB_CHUNKS) == TILES
EMB_STARTS = [sum(EMB_CHUNKS[:c]) for c in range(len(EMB_CHUNKS))]

HALF = B // 2
COLS = [(0, 128), (128, 256), (256, 384), (384, 512)]
ON_DVE = [True, False, False, False]
CENTRED_FIRST = 2
BC = B // P

WARM_START = 8
WARM_LAYER = [1, 3, 3, 6]

COL_W = 0
COL_FCW = COL_W + L * D
COL_B0 = COL_FCW + OUT
COL_GAMMA = COL_B0 + 1
COL_BETA = COL_GAMMA + L
PARAM_COLS = COL_BETA + L


def build(nc, x_main, x_short, emb_tiles, params, bias_rows, out):
    f32, i32, bf16 = mybir.dt.float32, mybir.dt.int32, mybir.dt.bfloat16
    ALU = mybir.AluOpType
    ACT = mybir.ActivationFunctionType
    PARTS = len(COLS)

    emb_chunk = [c for c, n in enumerate(EMB_CHUNKS) for _ in range(n)]

    def rows(t):
        return SHORT_ROWS if t == 0 else P

    ctx = ExitStack()
    with ctx:
        def sbuf(name, shape, dt=f32):
            return ctx.enter_context(nc.sbuf_tensor(name, shape, dt))

        def bank(name):
            return ctx.enter_context(nc.psum_tensor(name, [P, 512], f32))

        def sem(name):
            return ctx.enter_context(nc.semaphore(name))

        x_int = sbuf("x_int", [P, TILES, B], i32)
        x_f32 = sbuf("x_f32", [P, TILES, B])
        emb_sb = sbuf("emb_sb", [P, TILES, D])
        params_sb = sbuf("params_sb", [D, PARAM_COLS])
        b_rows = sbuf("b_rows", [1, COL_B0])
        emb_sum = sbuf("emb_sum", [D, B])
        h_sb = sbuf("h_sb", [D, L, B])
        centred = sbuf("centred", [D, L, B])
        stats = sbuf("stats", [D, L, PARTS, 6])
        moments = sbuf("moments", [D, L, 2])
        std = sbuf("std", [D, L])
        rstd = sbuf("rstd", [D, L])
        w_gamma = sbuf("w_gamma", [D, COL_B0])
        w_scaled = sbuf("w_scaled", [D, COL_B0])
        bias_sb = sbuf("bias_sb", [1, COL_B0])
        y_sb = sbuf("y_sb", [P, BC * OUT])
        scratch = sbuf("scratch", [P, 1])

        z = [bank(f"z{j}") for j in range(PARTS)]
        acc = z[-2:]
        ps_bias = [bank("ps_bias0"), bank("ps_bias1")]
        ps_warm = bank("ps_warm")
        ps_y = bank("ps_y")

        x_loaded = [sem(f"x_loaded{c}") for c in range(TILES)]
        emb_loaded = [sem(f"emb_loaded{c}") for c in range(len(EMB_CHUNKS))]
        params_loaded = sem("params_loaded")
        b_loaded = sem("b_loaded")
        x_cast = sem("x_cast")
        acc_done = [sem("acc_done0"), sem("acc_done1")]
        sum_copied = [sem(f"sum_copied{j}") for j in range(PARTS)]
        gamma_ready = sem("gamma_ready")
        z_done = [sem(f"z_done{j}") for j in range(PARTS)]
        relu_done = [sem(f"relu_done{j}") for j in range(PARTS)]
        stats_done = sem("stats_done")
        moments_done = sem("moments_done")
        centred_done = sem("centred_done")
        std_done = sem("std_done")
        rstd_done = sem("rstd_done")
        w_ready = sem("w_ready")
        bias_product = sem("bias_product")
        bias_ready = sem("bias_ready")
        y_product = sem("y_product")
        y_ready = sem("y_ready")
        out_stored = sem("out_stored")

        def weight_cols(layer):
            return ((layer + 1) * D, (layer + 2) * D) if layer < L - 1 else (COL_FCW, COL_FCW + OUT)

        def param(col, layer):
            return params_sb[:, col + layer:col + layer + 1]

        rows_made = [[0, 1], [2], [3], []]

        ones = nc.const_aps.tensor(1.0, [P, 512], bf16)
        ones_f32 = nc.const_aps.tensor(1.0, [1, 512], f32)

        block = ctx.enter_context(nc.Block())

        @block.sync
        def _(sp):
            for t in range(TILES):
                if t == 0:
                    sp.dma_start(x_int[0:SHORT_ROWS, 0, :], x_short[:, :]).then_inc(x_loaded[0], 16)
                if t in EMB_STARTS:
                    c = EMB_STARTS.index(t)
                    n = EMB_CHUNKS[c]
                    sp.dma_start(emb_sb[:, t:t + n, :], emb_tiles[:, t:t + n, :]).then_inc(emb_loaded[c], 16)
                if t > 0:
                    sp.dma_start(x_int[:, t, :], x_main[:, t - 1, :]).then_inc(x_loaded[t], 16)
            sp.dma_start(params_sb[:, :], params[:, :]).then_inc(params_loaded, 16)
            sp.dma_start(b_rows[:, D:], bias_rows[:, :]).then_inc(b_loaded, 16)

        @block.gpsimd
        def _(pool):
            pool.wait_ge(params_loaded, 16)
            for layer in range(L):
                a, b = weight_cols(layer)
                nc.gpsimd.tensor_scalar(w_gamma[:, a:b], params_sb[:, a:b], param(COL_GAMMA, layer), None,
                                        ALU.mult).then_inc(gamma_ready, 1)

        @block.scalar
        def _(act):
            nc.scalar.activation(scratch[:, :], nc.const_aps.tensor(1.0, [P, 1], f32), ACT.Sqrt)

            for j, (a, b) in enumerate(COLS):
                half = a // HALF
                act.wait_ge(acc_done[half], 1)
                nc.scalar.activation(emb_sum[:, a:b], acc[half][:, a % HALF:a % HALF + b - a],
                                     ACT.Copy).then_inc(sum_copied[j], 1)

            act.wait_ge(params_loaded, 16)
            for layer in range(L):
                for j, (a, b) in enumerate(COLS):
                    if not ON_DVE[j]:
                        act.wait_ge(z_done[j], layer + 1)
                        nc.scalar.activation(h_sb[:, layer, a:b], z[j][:, 0:b - a], ACT.Relu,
                                             bias=param(COL_B0, 0) if layer == 0 else 0.0).then_inc(relu_done[j], 1)
                for n in rows_made[layer]:
                    a, b = weight_cols(n)
                    act.wait_ge(bias_product, n + 1)
                    nc.scalar.activation(bias_sb[:, a:b], ps_bias[n % 2][0:1, 0:b - a], ACT.Copy).then_inc(bias_ready, 1)
                act.wait_ge(moments_done, layer + 1)
                nc.scalar.activation(std[:, layer:layer + 1], moments[:, layer, 1:2], ACT.Sqrt,
                                     bias=EPS).then_inc(std_done, 1)

            act.wait_ge(y_product, 1)
            nc.scalar.activation(y_sb[:, :], ps_y[:, 0:BC * OUT], ACT.Copy).then_inc(y_ready, 1)
            act.wait_ge(y_ready, 1)
            act.dma_start(out.rearrange("(p c) n -> p (c n)", c=BC), y_sb[:, :]).then_inc(out_stored, 16)
            act.wait_ge(out_stored, 16)

        @block.vector
        def _(dve):
            for t in range(TILES):
                dve.wait_ge(x_loaded[t], 16)
                for a, b in [(0, HALF), (HALF, B)] if t == TILES - 1 else [(0, B)]:
                    nc.vector.tensor_copy(x_f32[0:rows(t), t, a:b], x_int[0:rows(t), t, a:b]).then_inc(x_cast, 1)

            def centre(layer, a, b):
                nc.vector.tensor_scalar(centred[:, layer, a:b], h_sb[:, layer, a:b], moments[:, layer, 0:1], None,
                                        ALU.subtract).then_inc(centred_done, 1)

            dve.wait_ge(params_loaded, 16)
            for layer in range(L):
                for j, (a, b) in enumerate(COLS):
                    if ON_DVE[j]:
                        dve.wait_ge(z_done[j], layer + 1)
                        if layer == 0:
                            relu = nc.vector.tensor_scalar(h_sb[:, layer, a:b], z[j][:, 0:b - a], param(COL_B0, 0), 0.0,
                                                           ALU.add, ALU.max)
                        else:
                            relu = nc.vector.tensor_scalar(h_sb[:, layer, a:b], z[j][:, 0:b - a], 0.0, None, ALU.max)
                        relu.then_inc(relu_done[j], 1)
                for j, (a, b) in enumerate(COLS):
                    dve.wait_ge(relu_done[j], layer + 1)
                    nc.vector.bn_stats(stats[:, layer, j, :], h_sb[:, layer, a:b]).then_inc(stats_done, 1)
                dve.wait_ge(stats_done, PARTS * (layer + 1))
                nc.vector.bn_aggr(moments[:, layer, :], stats[:, layer, :, :]).then_inc(moments_done, 1)
                dve.wait_ge(moments_done, layer + 1)
                centre(layer, 0, COLS[CENTRED_FIRST][0])
                dve.wait_ge(std_done, layer + 1)
                nc.vector.reciprocal(rstd[:, layer:layer + 1], std[:, layer:layer + 1]).then_inc(rstd_done, 1)
                dve.wait_ge(rstd_done, layer + 1)
                dve.wait_ge(gamma_ready, layer + 1)
                a, b = weight_cols(layer)
                nc.vector.tensor_scalar(w_scaled[:, a:b], w_gamma[:, a:b], rstd[:, layer:layer + 1], None,
                                        ALU.mult).then_inc(w_ready, 1)
                centre(layer, COLS[CENTRED_FIRST][0], B)

        @block.tensor
        def _(pe):
            def keep_warm(n):
                for _ in range(n):
                    nc.tensor.matmul(ps_warm[:, :], ones[:, 0:P], ones,
                                     start=True, stop=True)

            def bias_row(n):
                a, b = weight_cols(n)
                if n >= 2:
                    pe.wait_ge(bias_ready, n - 1)
                nc.tensor.matmul(ps_bias[n % 2][0:1, 0:b - a], param(COL_BETA, n), params_sb[:, a:b],
                                 start=True, stop=False)
                nc.tensor.matmul(ps_bias[n % 2][0:1, 0:b - a], ones_f32[:, 0:1], b_rows[:, a:b],
                                 start=False, stop=True).then_inc(bias_product, 1)

            keep_warm(WARM_START)

            for t in range(TILES):
                pe.wait_ge(x_cast, t + 1)
                pe.wait_ge(emb_loaded[emb_chunk[t]], 16)
                for half in range(2):
                    if t == TILES - 1:
                        pe.wait_ge(x_cast, t + 1 + half)
                    done = nc.tensor.matmul(acc[half][:, 0:HALF], emb_sb[0:rows(t), t, :],
                                            x_f32[0:rows(t), t, half * HALF:(half + 1) * HALF],
                                            start=t == 0, stop=t == TILES - 1)
                    if t == TILES - 1:
                        done.then_inc(acc_done[half], 1)

            for layer in range(L):
                if layer == 0:
                    pe.wait_ge(params_loaded, 16)
                    weights, source = params_sb[:, COL_W:COL_W + D], emb_sum
                else:
                    a, b = weight_cols(layer - 1)
                    weights, source = w_scaled[:, a:b], centred[:, layer - 1, :]
                    pe.wait_ge(centred_done, 2 * layer - 1)
                    pe.wait_ge(w_ready, layer)
                for j, (a, b) in enumerate(COLS):
                    if layer == 0:
                        pe.wait_ge(sum_copied[j], 1)
                    elif j == CENTRED_FIRST:
                        pe.wait_ge(centred_done, 2 * layer)
                    nc.tensor.matmul(z[j][:, 0:b - a], weights, source[:, a:b],
                                     start=layer == 0, stop=True).then_inc(z_done[j], 1)
                if layer == 0:
                    pe.wait_ge(b_loaded, 16)
                for n in rows_made[layer]:
                    bias_row(n)
                pe.wait_ge(bias_ready, layer + 1)
                a, b = weight_cols(layer)
                if layer < L - 1:
                    row = bias_sb[:, a:b]
                    for j, (a, b) in enumerate(COLS):
                        pe.wait_ge(relu_done[j], layer + 1)
                        nc.tensor.matmul(z[j][:, 0:b - a], row, ones_f32[:, 0:b - a], start=True, stop=False)
                else:
                    nc.tensor.matmul(ps_y[:, 0:BC * OUT], ones_f32[:, 0:P],
                                     bias_sb[:, a:b].unsqueeze(1).broadcast_to([1, BC, OUT]), start=True, stop=False)
                keep_warm(WARM_LAYER[layer])

            pe.wait_ge(centred_done, 2 * L - 1)
            pe.wait_ge(w_ready, L)
            for c in range(BC):
                if (c + 1) * P > COLS[CENTRED_FIRST][0]:
                    pe.wait_ge(centred_done, 2 * L)
                done = nc.tensor.matmul(ps_y[:, c * OUT:(c + 1) * OUT], centred[:, L - 1, c * P:(c + 1) * P],
                                        w_scaled[:, COL_FCW:COL_FCW + OUT], start=False, stop=c == BC - 1)
            done.then_inc(y_product, 1)


def kernel(r_x, L0_rec_emb, L0_rec_Ws, L0_rec_bs, L0_rec_gammas, L0_rec_betas, L0_rec_fcW, L0_rec_fcb):
    import concourse.bacc as bacc
    from concourse.bass_utils import run_bass_kernel_spmd

    x_t = np.asarray(r_x).reshape(P, BC, V).transpose(2, 1, 0).reshape(V, B)
    emb, ws = np.asarray(L0_rec_emb), np.asarray(L0_rec_Ws)
    emb_short = np.pad(emb[FULL * P:], ((0, P - REST), (0, 0)))
    arrays = {
        "x_main": x_t[:FULL * P].reshape(P, FULL, B),
        "x_short": np.pad(x_t[FULL * P:], ((0, SHORT_ROWS - REST), (0, 0))),
        "emb_tiles": np.concatenate([emb_short[:, None, :], emb[:FULL * P].reshape(P, FULL, D)], axis=1),
        "params": np.concatenate(
            [ws.transpose(1, 0, 2).reshape(D, L * D), np.asarray(L0_rec_fcW), np.asarray(L0_rec_bs)[:1].T,
             np.asarray(L0_rec_gammas).T, np.asarray(L0_rec_betas).T], axis=1),
        "bias_rows": np.concatenate([np.asarray(L0_rec_bs)[1:].reshape(-1), np.asarray(L0_rec_fcb)])[None, :],
    }
    arrays = {name: np.ascontiguousarray(a) for name, a in arrays.items()}
    nc = bacc.Bacc("TRN2", target_bir_lowering=False, num_devices=1)
    ins = {name: nc.dram_tensor(name, a.shape, mybir.dt.from_np(a.dtype), kind="ExternalInput").ap()
           for name, a in arrays.items()}
    out = nc.dram_tensor("out", (B, OUT), mybir.dt.float32, kind="ExternalOutput").ap()
    build(nc, out=out, **ins)
    result = run_bass_kernel_spmd(nc, [arrays], core_ids=[0])
    return result.results[0]["out"]
```
